# Optimizing a Trainium2 kernel written in Bass

```python
import numpy as np
import jax
import jax.numpy as jnp

def _softmax(x, axis=-1):
    return jax.nn.softmax(x, axis=axis)

def _gelu(x):
    return jax.nn.gelu(x, approximate=True)

def _silu(x):
    return jax.nn.silu(x)

def _sigmoid(x):
    return jax.nn.sigmoid(x)

def _layernorm(x, axis=-1, eps=1e-05):
    m = jnp.mean(x, axis=axis, keepdims=True)
    v = jnp.var(x, axis=axis, keepdims=True)
    return (x - m) / jnp.sqrt(v + eps)

def _scatter_add(tgt, idx, src, axis=0):
    return tgt.at[idx].add(src)

def _segment_sum(src, seg, n):
    return jax.ops.segment_sum(src, seg, n)
kernel_name = 'mk_dlrm_tower_d1_rec_r8_c52220'

def setup_inputs(seed: int=0):
    np.random.seed(seed)
    _w = jnp.asarray

    def _rec_inputs():
        import jax
        import jax.numpy as jnp
        _tk = jax.random.key(seed)
        ids = jnp.stack([jax.random.randint(jax.random.fold_in(_tk, 200 + f), (512,), 0, v, jnp.int32) for f, v in enumerate([1000, 1000, 1250, 125000, 12500, 12500, 1000, 1000, 12500, 12500, 12500, 12500, 12500, 1250, 12500, 1250, 12500, 1250, 1000, 1000, 1000, 1000, 1000, 1000, 1000, 1000])], axis=1)
        tbl_0 = 0.05 * jax.random.normal(jax.random.fold_in(_tk, 500 + 0), (1000, 128), jnp.float32)
        tbl_1 = 0.05 * jax.random.normal(jax.random.fold_in(_tk, 500 + 1), (1000, 128), jnp.float32)
        tbl_2 = 0.05 * jax.random.normal(jax.random.fold_in(_tk, 500 + 2), (1250, 128), jnp.float32)
        tbl_3 = 0.05 * jax.random.normal(jax.random.fold_in(_tk, 500 + 3), (125000, 128), jnp.float32)
        tbl_4 = 0.05 * jax.random.normal(jax.random.fold_in(_tk, 500 + 4), (12500, 128), jnp.float32)
        tbl_5 = 0.05 * jax.random.normal(jax.random.fold_in(_tk, 500 + 5), (12500, 128), jnp.float32)
        tbl_6 = 0.05 * jax.random.normal(jax.random.fold_in(_tk, 500 + 6), (1000, 128), jnp.float32)
        tbl_7 = 0.05 * jax.random.normal(jax.random.fold_in(_tk, 500 + 7), (1000, 128), jnp.float32)
        tbl_8 = 0.05 * jax.random.normal(jax.random.fold_in(_tk, 500 + 8), (12500, 128), jnp.float32)
        tbl_9 = 0.05 * jax.random.normal(jax.random.fold_in(_tk, 500 + 9), (12500, 128), jnp.float32)
        tbl_10 = 0.05 * jax.random.normal(jax.random.fold_in(_tk, 500 + 10), (12500, 128), jnp.float32)
        tbl_11 = 0.05 * jax.random.normal(jax.random.fold_in(_tk, 500 + 11), (12500, 128), jnp.float32)
        tbl_12 = 0.05 * jax.random.normal(jax.random.fold_in(_tk, 500 + 12), (12500, 128), jnp.float32)
        tbl_13 = 0.05 * jax.random.normal(jax.random.fold_in(_tk, 500 + 13), (1250, 128), jnp.float32)
        tbl_14 = 0.05 * jax.random.normal(jax.random.fold_in(_tk, 500 + 14), (12500, 128), jnp.float32)
        tbl_15 = 0.05 * jax.random.normal(jax.random.fold_in(_tk, 500 + 15), (1250, 128), jnp.float32)
        tbl_16 = 0.05 * jax.random.normal(jax.random.fold_in(_tk, 500 + 16), (12500, 128), jnp.float32)
        tbl_17 = 0.05 * jax.random.normal(jax.random.fold_in(_tk, 500 + 17), (1250, 128), jnp.float32)
        tbl_18 = 0.05 * jax.random.normal(jax.random.fold_in(_tk, 500 + 18), (1000, 128), jnp.float32)
        tbl_19 = 0.05 * jax.random.normal(jax.random.fold_in(_tk, 500 + 19), (1000, 128), jnp.float32)
        tbl_20 = 0.05 * jax.random.normal(jax.random.fold_in(_tk, 500 + 20), (1000, 128), jnp.float32)
        tbl_21 = 0.05 * jax.random.normal(jax.random.fold_in(_tk, 500 + 21), (1000, 128), jnp.float32)
        tbl_22 = 0.05 * jax.random.normal(jax.random.fold_in(_tk, 500 + 22), (1000, 128), jnp.float32)
        tbl_23 = 0.05 * jax.random.normal(jax.random.fold_in(_tk, 500 + 23), (1000, 128), jnp.float32)
        tbl_24 = 0.05 * jax.random.normal(jax.random.fold_in(_tk, 500 + 24), (1000, 128), jnp.float32)
        tbl_25 = 0.05 * jax.random.normal(jax.random.fold_in(_tk, 500 + 25), (1000, 128), jnp.float32)
        _rk = jax.random.fold_in(_tk, 7)
        r_dense_proj = -0.000520686 + 1.00062 * jax.random.normal(jax.random.fold_in(_rk, 101), (512, 128), jnp.float32)
        W_top1 = 0.0405887 * jax.random.normal(jax.random.fold_in(_tk, 801), (607, 512), jnp.float32)
        W_top2 = 0.0441942 * jax.random.normal(jax.random.fold_in(_tk, 802), (512, 256), jnp.float32)
        W_top3 = 0.0625 * jax.random.normal(jax.random.fold_in(_tk, 803), (256, 1), jnp.float32)
        b_top1 = jnp.zeros((512,), jnp.float32)
        b_top2 = jnp.zeros((256,), jnp.float32)
        return (r_dense_proj, ids, tbl_0, tbl_1, tbl_2, tbl_3, tbl_4, tbl_5, tbl_6, tbl_7, tbl_8, tbl_9, tbl_10, tbl_11, tbl_12, tbl_13, tbl_14, tbl_15, tbl_16, tbl_17, tbl_18, tbl_19, tbl_20, tbl_21, tbl_22, tbl_23, tbl_24, tbl_25, W_top1, b_top1, W_top2, b_top2, W_top3)
    r_dense_proj, ids, tbl_0, tbl_1, tbl_2, tbl_3, tbl_4, tbl_5, tbl_6, tbl_7, tbl_8, tbl_9, tbl_10, tbl_11, tbl_12, tbl_13, tbl_14, tbl_15, tbl_16, tbl_17, tbl_18, tbl_19, tbl_20, tbl_21, tbl_22, tbl_23, tbl_24, tbl_25, W_top1, b_top1, W_top2, b_top2, W_top3 = _rec_inputs()

    def _L0_rec_setup():
        import jax, jax.numpy as jnp
        import numpy as np
        key = jax.random.key(seed)
        k1, k2 = jax.random.split(key)
        B, N_SPARSE, D = (2048, 26, 128)
        dense_proj = jax.random.normal(k1, (B, D), dtype=jnp.float32)
        sparse_embs = jax.random.normal(k2, (B, N_SPARSE, D), dtype=jnp.float32)
        return {'dense_proj': dense_proj, 'sparse_embs': sparse_embs}
    _L0_rec_all = _L0_rec_setup()
    _L0_rec_in = {k: v for k, v in _L0_rec_all.items() if k in ()}
    del _L0_rec_all
    return {'r_dense_proj': r_dense_proj, 'ids': ids, 'tbl_0': tbl_0, 'tbl_1': tbl_1, 'tbl_2': tbl_2, 'tbl_3': tbl_3, 'tbl_4': tbl_4, 'tbl_5': tbl_5, 'tbl_6': tbl_6, 'tbl_7': tbl_7, 'tbl_8': tbl_8, 'tbl_9': tbl_9, 'tbl_10': tbl_10, 'tbl_11': tbl_11, 'tbl_12': tbl_12, 'tbl_13': tbl_13, 'tbl_14': tbl_14, 'tbl_15': tbl_15, 'tbl_16': tbl_16, 'tbl_17': tbl_17, 'tbl_18': tbl_18, 'tbl_19': tbl_19, 'tbl_20': tbl_20, 'tbl_21': tbl_21, 'tbl_22': tbl_22, 'tbl_23': tbl_23, 'tbl_24': tbl_24, 'tbl_25': tbl_25, 'W_top1': W_top1, 'b_top1': b_top1, 'W_top2': W_top2, 'b_top2': b_top2, 'W_top3': W_top3}

def reference(r_dense_proj, ids, tbl_0, tbl_1, tbl_2, tbl_3, tbl_4, tbl_5, tbl_6, tbl_7, tbl_8, tbl_9, tbl_10, tbl_11, tbl_12, tbl_13, tbl_14, tbl_15, tbl_16, tbl_17, tbl_18, tbl_19, tbl_20, tbl_21, tbl_22, tbl_23, tbl_24, tbl_25, W_top1, b_top1, W_top2, b_top2, W_top3):
    import jax
    import jax.numpy as jnp

    def _L0_rec_ref(dense_proj, sparse_embs):
        import jax, jax.numpy as jnp
        import numpy as np
        all_vecs = jnp.concatenate([dense_proj[:, None, :], sparse_embs], axis=1)
        n = all_vecs.shape[1]
        interactions = jnp.einsum('bnd,bmd->bnm', all_vecs, all_vecs)
        rows, cols = np.triu_indices(n, k=1)
        interact_flat = interactions[:, rows, cols]
        return jnp.concatenate([dense_proj, interact_flat], axis=1)
    e = jnp.stack([tbl_0[ids[:, 0]], tbl_1[ids[:, 1]], tbl_2[ids[:, 2]], tbl_3[ids[:, 3]], tbl_4[ids[:, 4]], tbl_5[ids[:, 5]], tbl_6[ids[:, 6]], tbl_7[ids[:, 7]], tbl_8[ids[:, 8]], tbl_9[ids[:, 9]], tbl_10[ids[:, 10]], tbl_11[ids[:, 11]], tbl_12[ids[:, 12]], tbl_13[ids[:, 13]], tbl_14[ids[:, 14]], tbl_15[ids[:, 15]], tbl_16[ids[:, 16]], tbl_17[ids[:, 17]], tbl_18[ids[:, 18]], tbl_19[ids[:, 19]], tbl_20[ids[:, 20]], tbl_21[ids[:, 21]], tbl_22[ids[:, 22]], tbl_23[ids[:, 23]], tbl_24[ids[:, 24]], tbl_25[ids[:, 25]]], axis=1)
    z = _L0_rec_ref(r_dense_proj, e)
    z = z.reshape(z.shape[0], -1)
    h = jnp.concatenate([z, r_dense_proj], axis=1)
    h = jnp.maximum(h @ W_top1 + b_top1, 0.0)
    h = jnp.maximum(h @ W_top2 + b_top2, 0.0)
    y = h @ W_top3
    return y

_drawn_inputs = setup_inputs


def setup_inputs(seed=0):
    import zlib

    import numpy as np

    out = dict(_drawn_inputs(seed))
    spreads = {'b_top1': (0.0, 0.1), 'b_top2': (0.0, 0.1)}
    factors = {}
    for name, (base, spread) in spreads.items():
        noise = np.random.default_rng([zlib.crc32(name.encode()), seed]).standard_normal(out[name].shape)
        drawn = base * np.exp(spread * noise) if base else spread * noise
        out[name] = jnp.asarray(drawn.astype(out[name].dtype))
    for name, factor in factors.items():
        out[name] = (out[name] * factor).astype(out[name].dtype)
    return out
```

```python
import concourse.bass as bass
from concourse import mybir
from contextlib import ExitStack

BATCH = 512
DIM = 128
TABLES = 26
VECS = TABLES + 1
TILES = BATCH // 128
HID1 = 512
HID2 = 256
S1 = HID1 // 128
S2 = HID2 // 128
QUADS = 4
PER_QUAD = -(-TABLES // QUADS)
GROUPS = [(v, min(4, VECS - v)) for v in range(1, VECS, 4)]


def build_dlrm(nc, a, y_out):
    fp32 = mybir.dt.float32
    i32 = mybir.dt.int32
    ALU = mybir.AluOpType
    ACT = mybir.ActivationFunctionType

    ctx = ExitStack()
    with ctx:
        def sb(name, shape, dt=fp32):
            return ctx.enter_context(nc.sbuf_tensor(name, shape, dt))

        def bank(name):
            return ctx.enter_context(nc.psum_tensor(name, [128, 512], fp32))

        def sem(name):
            return ctx.enter_context(nc.semaphore(name))

        ids = sb("ids", [128, TILES, TABLES], i32)
        rows = [sb(f"rows{i}", [128, TABLES, DIM]) for i in range(2)]
        vecs = sb("vecs", [128, 128, VECS])
        dense = sb("dense", [128, BATCH])
        pairs = sb("pairs", [128, PER_QUAD, BATCH])
        w1 = sb("w1", [128, PER_QUAD, HID1])
        w1_dense2 = sb("w1_dense2", [128, 2, HID1])
        w1_dense = sb("w1_dense", [128, HID1])
        w2 = sb("w2", [128, S1, HID2])
        w3 = sb("w3", [128, S2])
        b1 = sb("b1", [128, S1])
        b2 = sb("b2", [128, S2])
        identity = sb("identity", [128, 128])
        h1 = sb("h1", [128, S1, 128])
        h2 = sb("h2", [128, S2, 128])
        y = sb("y", [1, BATCH])

        turned = [bank(f"turned{i}") for i in range(2)]
        gram = ctx.enter_context(nc.psum_tensor("gram", [128, 2, 512], fp32))
        h1_sum = bank("h1_sum")
        h2_sum = bank("h2_sum")
        y_sum = bank("y_sum")

        ids_in = sem("ids_in")
        dense_in = sem("dense_in")
        w1_in = sem("w1_in")
        w1d_in = sem("w1d_in")
        w2_in = sem("w2_in")
        small_in = sem("small_in")
        rows_in = [[sem(f"rows_in{i}_{g}") for g in range(len(GROUPS))] for i in range(2)]
        ident_zero = sem("ident_zero")
        ident_ready = sem("ident_ready")
        pairs_zero = sem("pairs_zero")
        w1_dense_ready = sem("w1_dense_ready")
        turned_ready = sem("turned_ready")
        vecs_ready_act = sem("vecs_ready_act")
        vecs_ready_dve = sem("vecs_ready_dve")
        dense_placed = sem("dense_placed")
        gram_ready = sem("gram_ready")
        pairs_ready_act = sem("pairs_ready_act")
        pairs_ready_dve = sem("pairs_ready_dve")
        h1_sum_ready = sem("h1_sum_ready")
        h1_ready = sem("h1_ready")
        h2_sum_ready = sem("h2_sum_ready")
        h2_ready = sem("h2_ready")
        y_sum_ready = sem("y_sum_ready")
        y_ready = sem("y_ready")
        y_stored = sem("y_stored")

        NG = len(GROUPS)
        NA = sum(1 for g in range(NG) if g % 2 == 0)
        ND = NG - NA
        def copied(k):
            t, g = divmod(k, NG)
            return t * NA + (g + 1) // 2, t * ND + g // 2

        block = ctx.enter_context(nc.Block())

        @block.sync
        def _(sp):
            sp.dma_start(ids[:, :, :], a["ids"]).then_inc(ids_in, 16)
            sp.dma_start(dense[:, :], a["dense_t"]).then_inc(dense_in, 16)
            sp.dma_start(w1_dense2[:, :, :], a["w1_dense"]).then_inc(w1d_in, 16)
            sp.dma_start(w1[:, :, :], a["w1_pairs"]).then_inc(w1_in, 16)
            sp.dma_start(w2[:, :, :], a["w2"]).then_inc(w2_in, 16)
            sp.dma_start(b1[:, :], a["b1"]).then_inc(small_in, 16)
            sp.dma_start(b2[:, :], a["b2"]).then_inc(small_in, 16)
            sp.dma_start(w3[:, :], a["w3"]).then_inc(small_in, 16)
            sp.wait_ge(y_ready, TILES)
            sp.dma_start(y_out, y[:, :]).then_inc(y_stored, 16)
            sp.wait_ge(y_stored, 16)

        @block.gpsimd
        def _(pool):
            nc.gpsimd.memset(identity[:, :], 0.0).then_inc(ident_zero, 1)
            pool.wait_ge(ident_zero, 1)
            nc.gpsimd.affine_select(out=identity[:, :], in_=identity[:, :], compare_op=ALU.not_equal,
                                    fill=1.0, base=0, pattern=[[-1, 128]],
                                    channel_multiplier=1).then_inc(ident_ready, 1)
            pool.wait_ge(ids_in, 16)
            for t in range(TILES):
                for g, (v0, n) in enumerate(GROUPS):
                    if t >= 2:
                        pool.wait_ge(turned_ready, NG * (t - 2) + g + 1)
                    for f in range(v0 - 1, v0 - 1 + n):
                        pool.indirect_dma_start(
                            rows[t % 2][:, f, :], None, a[f"tbl_{f}"],
                            bass.IndirectOffsetOnAxis(ids[:, t, f:f + 1], 0)).then_inc(rows_in[t % 2][g], 16)

        @block.tensor
        def _(pe):
            pe.wait_ge(ident_ready, 1)
            for t in range(TILES):
                for g, (v0, n) in enumerate(GROUPS):
                    pe.wait_ge(rows_in[t % 2][g], 16 * n * (t // 2 + 1))
                    k = t * NG + g
                    if k >= 2:
                        pe.wait_ge(vecs_ready_act, copied(k - 1)[0])
                        pe.wait_ge(vecs_ready_dve, copied(k - 1)[1])
                    for u in range(n):
                        last = nc.tensor.transpose(turned[k % 2][:, u * 128:(u + 1) * 128],
                                                   rows[t % 2][:, v0 - 1 + u, :], identity[:, :])
                    last.then_inc(turned_ready, 1)
                pe.wait_ge(vecs_ready_act, copied((t + 1) * NG)[0])
                pe.wait_ge(vecs_ready_dve, copied((t + 1) * NG)[1])
                pe.wait_ge(dense_placed, t + 1)
                if t >= 1:
                    pe.wait_ge(pairs_ready_act, t)
                    pe.wait_ge(pairs_ready_dve, t)
                for i in range(32):
                    for j in range(QUADS):
                        x = vecs[:, 32 * j + i, :]
                        last = nc.tensor.matmul(
                            gram[32 * j:32 * j + VECS, i // 16, (i % 16) * VECS:(i % 16 + 1) * VECS],
                            x, x, start=True, stop=True)
                last.then_inc(gram_ready, 1)
                cols = slice(t * 128, (t + 1) * 128)
                if t == 0:
                    pe.wait_ge(w1_dense_ready, 1)
                    pe.wait_ge(w1_in, 16)
                pe.wait_ge(pairs_ready_act, t + 1)
                pe.wait_ge(pairs_ready_dve, t + 1)
                for s in range(S1):
                    o = slice(s * 128, (s + 1) * 128)
                    nc.tensor.matmul(h1_sum[:, o], w1_dense[:, o], dense[:, cols], start=True, stop=False)
                    for c in range(PER_QUAD):
                        last = nc.tensor.matmul(h1_sum[:, o], w1[:, c, o], pairs[:, c, cols],
                                                start=False, stop=c == PER_QUAD - 1)
                last.then_inc(h1_sum_ready, 1)
                if t == 0:
                    pe.wait_ge(w2_in, 16)
                pe.wait_ge(h1_ready, t + 1)
                for o in range(S2):
                    for s in range(S1):
                        last = nc.tensor.matmul(h2_sum[:, o * 128:(o + 1) * 128],
                                                w2[:, s, o * 128:(o + 1) * 128], h1[:, s, :],
                                                start=s == 0, stop=s == S1 - 1)
                last.then_inc(h2_sum_ready, 1)
                if t == 0:
                    pe.wait_ge(small_in, 48)
                pe.wait_ge(h2_ready, t + 1)
                for o in range(S2):
                    last = nc.tensor.matmul(y_sum[0:1, 0:128], w3[:, o:o + 1], h2[:, o, :],
                                            start=o == 0, stop=o == S2 - 1)
                last.then_inc(y_sum_ready, 1)

        def place_pairs(copy, t, j, quads):
            for q in quads:
                nm = min(PER_QUAD, TABLES - PER_QUAD * q)
                src = gram[32 * j:32 * j + VECS, :, 0:16 * VECS].rearrange("n h (i m) -> n m h i", m=VECS)
                m0 = 1 + PER_QUAD * q
                dst = pairs[32 * q:32 * q + VECS, 0:nm, t * 128 + 32 * j:t * 128 + 32 * j + 32]
                last = copy(dst.rearrange("n m (h i) -> n m h i", h=2), src[:, m0:m0 + nm, :, :])
            return last

        @block.scalar
        def _(act):
            for t in range(TILES):
                for g in range(0, NG, 2):
                    v0, n = GROUPS[g]
                    k = t * NG + g
                    if g == 0 and t >= 1:
                        act.wait_ge(gram_ready, t)
                    act.wait_ge(turned_ready, k + 1)
                    nc.scalar.copy(vecs[:, :, v0:v0 + n].rearrange("d b n -> d n b"),
                                   turned[k % 2][:, 0:n * 128].rearrange("d (n b) -> d n b", n=n)
                                   ).then_inc(vecs_ready_act, 1)
                act.wait_ge(gram_ready, t + 1)
                if t == 0:
                    act.wait_ge(pairs_zero, 1)
                for j in (0, 2):
                    last = place_pairs(nc.scalar.copy, t, j, range(QUADS))
                last.then_inc(pairs_ready_act, 1)
                if t == 0:
                    act.wait_ge(small_in, 48)
                act.wait_ge(h1_sum_ready, t + 1)
                for s in range(S1):
                    last = nc.scalar.activation(h1[:, s, :], h1_sum[:, s * 128:(s + 1) * 128], ACT.Relu,
                                                bias=b1[:, s:s + 1])
                last.then_inc(h1_ready, 1)

        @block.vector
        def _(dve):
            nc.vector.memset(pairs[:, :, :], 0.0).then_inc(pairs_zero, 1)
            dve.wait_ge(w1d_in, 16)
            nc.vector.tensor_tensor(w1_dense[:, :], w1_dense2[:, 0, :], w1_dense2[:, 1, :],
                                    ALU.add).then_inc(w1_dense_ready, 1)
            dve.wait_ge(dense_in, 16)
            dve.wait_ge(pairs_zero, 1)
            for t in range(TILES):
                if t >= 1:
                    dve.wait_ge(gram_ready, t)
                nc.vector.tensor_copy(vecs[:, :, 0], dense[:, t * 128:(t + 1) * 128]).then_inc(dense_placed, 1)
                for g in range(1, NG, 2):
                    v0, n = GROUPS[g]
                    k = t * NG + g
                    dve.wait_ge(turned_ready, k + 1)
                    nc.vector.tensor_copy(vecs[:, :, v0:v0 + n].rearrange("d b n -> d n b"),
                                          turned[k % 2][:, 0:n * 128].rearrange("d (n b) -> d n b", n=n)
                                          ).then_inc(vecs_ready_dve, 1)
                dve.wait_ge(gram_ready, t + 1)
                for j in (1, 3):
                    last = place_pairs(nc.vector.tensor_copy, t, j, range(QUADS))
                last.then_inc(pairs_ready_dve, 1)
                if t == 0:
                    dve.wait_ge(small_in, 48)
                dve.wait_ge(h2_sum_ready, t + 1)
                for o in range(S2):
                    last = nc.vector.tensor_scalar(h2[:, o, :], h2_sum[:, o * 128:(o + 1) * 128],
                                                   b2[:, o:o + 1], 0.0, ALU.add, ALU.max)
                last.then_inc(h2_ready, 1)
                dve.wait_ge(y_sum_ready, t + 1)
                nc.vector.tensor_copy(y[:, t * 128:(t + 1) * 128], y_sum[0:1, 0:128]).then_inc(y_ready, 1)


def kernel(**inputs):
    import numpy as _np
    import concourse.bacc as _bacc
    from concourse import mybir as _mybir
    from concourse.bass_utils import run_bass_kernel_spmd as _run

    x = {k: _np.asarray(v) for k, v in inputs.items()}
    W1 = x["W_top1"]
    n_pairs = VECS * (VECS - 1) // 2
    w1_pairs = _np.zeros((128, PER_QUAD, HID1), W1.dtype)
    k = DIM
    for n in range(VECS):
        for m in range(n + 1, VECS):
            q, c = divmod(m - 1, PER_QUAD)
            w1_pairs[32 * q + n, c] = W1[k]
            k += 1
    arrays = {
        "ids": x["ids"].reshape(TILES, 128, TABLES).transpose(1, 0, 2),
        "dense_t": x["r_dense_proj"].T,
        "w1_dense": _np.stack([W1[:DIM], W1[DIM + n_pairs:]], axis=1),
        "w1_pairs": w1_pairs,
        "w2": x["W_top2"].reshape(S1, 128, HID2).transpose(1, 0, 2),
        "w3": x["W_top3"].reshape(S2, 128).T,
        "b1": x["b_top1"].reshape(S1, 128).T,
        "b2": x["b_top2"].reshape(S2, 128).T,
    }
    for f in range(TABLES):
        arrays[f"tbl_{f}"] = x[f"tbl_{f}"]
    nc = _bacc.Bacc("TRN2", target_bir_lowering=False, num_devices=1)
    arrays = {k: _np.ascontiguousarray(v) for k, v in arrays.items()}
    aps = {k: nc.dram_tensor(f"in_{k}", v.shape, _mybir.dt.from_np(v.dtype), kind="ExternalInput").ap()
           for k, v in arrays.items()}
    y_out = nc.dram_tensor("out_y", (BATCH, 1), _mybir.dt.float32, kind="ExternalOutput").ap()
    build_dlrm(nc, aps, y_out.rearrange("b o -> o b"))
    r = _run(nc, [{f"in_{k}": v for k, v in arrays.items()}], core_ids=[0])
    return r.results[0]["out_y"]
```

```python
import concourse.bass as bass
from concourse import mybir
from contextlib import ExitStack

BATCH = 512
DIM = 128
TABLES = 26
VECS = TABLES + 1
TILE = 128
TILES = BATCH // TILE
HALF = TILE // 2
HID1 = 512
HID2 = 256
S1 = HID1 // 128
S2 = HID2 // 128
QUADS = 4
PER_QUAD = HALF // QUADS
CHUNKS = 4
LAYERS = [[(27, 23), (10, 7)],
          [(27, 0), (14, 11)],
          [(27, 4), (19, 15), (4, 0)],
          [(27, 8), (22, 19), (7, 3)]]
PICKED = 8
PICK_ROWS = 1000
PER_PART = 8
PICK_PARTS = PICK_ROWS // PER_PART
PIECE = PER_PART // 2
GATHERED = TABLES - PICKED
GROUPS = [(f, min(4, GATHERED - f)) for f in range(0, GATHERED, 4)]
NG = len(GROUPS)
WARM_UPS = 13
TURNS_AFTER = {2: [(0, 0)], 3: [(0, 1)], 4: [(0, 2), (0, 3)], 5: [(0, 4), (1, 0)], 6: [(1, 1)], 7: [(1, 2)]}
BATCHES = [(0, 256), (256, 128), (384, 128)]


def build_dlrm(nc, a, y_out):
    fp32 = mybir.dt.float32
    fp32r = mybir.dt.float32r
    fp16 = mybir.dt.float16
    bf16 = mybir.dt.bfloat16
    i32 = mybir.dt.int32
    ALU = mybir.AluOpType
    ACT = mybir.ActivationFunctionType

    ctx = ExitStack()
    with ctx:
        def sb(name, shape, dt=fp32):
            return ctx.enter_context(nc.sbuf_tensor(name, shape, dt))

        def bank(name):
            return ctx.enter_context(nc.psum_tensor(name, [128, 512], fp32))

        def sem(name):
            return ctx.enter_context(nc.semaphore(name))

        ids = sb("ids", [128, TILES, GATHERED], i32)
        rows = [sb(f"rows{i}", [128, GATHERED, DIM]) for i in range(2)]
        vecs = sb("vecs", [128, BATCH, VECS])
        dense = sb("dense", [128, BATCH])
        pairs = sb("pairs", [128, CHUNKS, BATCH])
        w1 = sb("w1", [128, CHUNKS, HID1])
        w1_dense = sb("w1_dense", [128, HID1])
        w1_dense2 = sb("w1_dense2", [128, 2, HID1])
        w2 = sb("w2", [128, S1, HID2])
        w3 = sb("w3", [128, S2])
        b1 = sb("b1", [128, S1])
        b2 = sb("b2", [128, S2])
        identity = sb("identity", [128, 128])
        h1 = sb("h1", [128, S1, 256])
        h2 = sb("h2", [128, S2, 256])
        y = sb("y", [1, BATCH])
        minus_first = sb("minus_first", [PICK_PARTS, 1])
        pick_ids = [sb(f"pick_ids{i}", [PICK_PARTS, BATCH], i32) for i in range(2)]
        offset = [sb(f"offset{i}", [PICK_PARTS, BATCH], fp16) for i in range(2)]
        table = [sb(f"table{i}", [PICK_PARTS, PER_PART, DIM]) for i in range(2)]
        table_hi = [sb(f"table_hi{i}", [PICK_PARTS, PER_PART, DIM], fp32r) for i in range(2)]
        table_lo = [sb(f"table_lo{i}", [PICK_PARTS, PER_PART, DIM], fp32r) for i in range(2)]
        distance = sb("distance", [PICK_PARTS, BATCH], fp16)
        warm = sb("warm", [1, 2])
        blank = sb("blank", [128, 512], bf16)
        one = sb("one", [PICK_PARTS, 1])
        minus_last = sb("minus_last", [PICK_PARTS, 1])
        onehot = [sb(f"onehot{i}", [PICK_PARTS, PIECE, BATCH], fp32r) for i in range(2)]

        turned = [bank(f"turned{i}") for i in range(2)]
        gram = [bank(f"gram{i}") for i in range(2)]
        shared = [bank(f"shared{i}") for i in range(2)]
        h2_sum = bank("h2_sum")
        y_sum = bank("y_sum")

        ids_in = sem("ids_in")
        first_in = sem("first_in")
        dense_in = sem("dense_in")
        w1_in = sem("w1_in")
        w1d_in = sem("w1d_in")
        w2_in = sem("w2_in")
        small_in = sem("small_in")
        pick_ids_in = [sem(f"pick_ids_in{i}") for i in range(2)]
        table_in = [sem(f"table_in{i}") for i in range(2)]
        rows_in = [[sem(f"rows_in{i}_{g}") for g in range(NG)] for i in range(2)]
        ident_zero = sem("ident_zero")
        ident_ready = sem("ident_ready")
        pairs_zero = sem("pairs_zero")
        w1_dense_ready = sem("w1_dense_ready")
        dense_placed = sem("dense_placed")
        table_hi_ready = sem("table_hi_ready")
        table_lo_ready = sem("table_lo_ready")
        offset_ready = sem("offset_ready")
        onehot_ready = sem("onehot_ready")
        distance_ready = sem("distance_ready")
        last_onehot_ready = sem("last_onehot_ready")
        warm_zero = sem("warm_zero")
        blank_zero = sem("blank_zero")
        piece_used = sem("piece_used")
        picked_placed = sem("picked_placed")
        turned_ready = sem("turned_ready")
        turned_placed = sem("turned_placed")
        gram_ready = sem("gram_ready")
        layer_act = sem("layer_act")
        layer_dve = sem("layer_dve")
        pairs_act = sem("pairs_act")
        pairs_dve = sem("pairs_dve")
        h1_sum_ready = sem("h1_sum_ready")
        h1_ready = sem("h1_ready")
        h2_sum_ready = sem("h2_sum_ready")
        h2_ready = sem("h2_ready")
        y_sum_ready = sem("y_sum_ready")
        y_ready = sem("y_ready")
        y_stored = sem("y_stored")

        block = ctx.enter_context(nc.Block())

        def load_pick_ids(eng, u):
            if u >= 2:
                eng.wait_ge(offset_ready, u - 1)
            eng.dma_start(pick_ids[u % 2][:, :], a["pick_ids"][u:u + 1, :].to_broadcast([PICK_PARTS, BATCH])
                          ).then_inc(pick_ids_in[u % 2], 16)

        def load_table(eng, u):
            if u >= 2:
                eng.wait_ge(table_hi_ready, u - 1)
                eng.wait_ge(table_lo_ready, u - 1)
            eng.dma_start(table[u % 2][:, :, :],
                          a[f"tbl_{GATHERED + u}"].rearrange("(p r) d -> p r d", r=PER_PART)
                          ).then_inc(table_in[u % 2], 16)

        @block.sync
        def _(sp):
            sp.dma_start(ids[:, :, :], a["ids"]).then_inc(ids_in, 16)
            load_table(sp, 0)
            load_pick_ids(sp, 1)
            load_table(sp, 1)
            sp.dma_start(dense[:, :], a["dense_t"]).then_inc(dense_in, 16)
            for u in range(2, PICKED):
                load_pick_ids(sp, u)
                load_table(sp, u)
            sp.dma_start(w1_dense2[:, :, :], a["w1_dense"]).then_inc(w1d_in, 16)
            sp.dma_start(w1[:, :, :], a["w1_pairs"]).then_inc(w1_in, 16)
            sp.dma_start(b1[:, :], a["b1"]).then_inc(small_in, 16)
            sp.dma_start(b2[:, :], a["b2"]).then_inc(small_in, 16)
            sp.dma_start(w3[:, :], a["w3"]).then_inc(small_in, 16)
            sp.dma_start(w2[:, :, :], a["w2"]).then_inc(w2_in, 16)
            sp.wait_ge(y_ready, len(BATCHES))
            sp.dma_start(y_out, y[:, :]).then_inc(y_stored, 16)
            sp.wait_ge(y_stored, 16)

        @block.gpsimd
        def _(pool):
            nc.gpsimd.memset(identity[:, :], 0.0).then_inc(ident_zero, 1)
            pool.wait_ge(ident_zero, 1)
            nc.gpsimd.affine_select(out=identity[:, :], in_=identity[:, :], compare_op=ALU.not_equal,
                                    fill=1.0, base=0, pattern=[[-1, 128]],
                                    channel_multiplier=1).then_inc(ident_ready, 1)
            pool.wait_ge(ids_in, 16)
            for t in range(TILES):
                for g, (f0, n) in enumerate(GROUPS):
                    if t >= 2:
                        pool.wait_ge(turned_ready, NG * (t - 2) + g + 1)
                    for f in range(f0, f0 + n):
                        pool.indirect_dma_start(
                            rows[t % 2][:, f, :], None, a[f"tbl_{f}"],
                            bass.IndirectOffsetOnAxis(ids[:, t, f:f + 1], 0)).then_inc(rows_in[t % 2][g], 16)

        @block.tensor
        def _(pe):
            def pick(u):
                if u >= 2:
                    pe.wait_ge(picked_placed, u - 1)
                for half in range(2):
                    for part in range(2):
                        if half == 0 and part == 0:
                            pe.wait_ge(table_hi_ready, u + 1)
                        if half == 0 and part == 1:
                            pe.wait_ge(table_lo_ready, u + 1)
                        side = (table_hi, table_lo)[part][u % 2]
                        for k in range(PIECE):
                            c = half * PIECE + k
                            if part == 0 and c < PER_PART - 1:
                                pe.wait_ge(onehot_ready, (PER_PART - 1) * u + c + 1)
                            elif part == 0:
                                pe.wait_ge(last_onehot_ready, u + 1)
                            last = nc.tensor.matmul(shared[u % 2][:, :], side[:, c, :], onehot[half][:, k, :],
                                                    start=c == 0 and part == 0,
                                                    stop=c == PER_PART - 1 and part == 1)
                    last.then_inc(piece_used, 1)

            def turn(t, g):
                k = t * NG + g
                f0, n = GROUPS[g]
                pe.wait_ge(rows_in[t % 2][g], 16 * n * (t // 2 + 1))
                if k >= 2:
                    pe.wait_ge(turned_placed, k - 1)
                for u in range(n):
                    last = nc.tensor.transpose(turned[k % 2][:, u * 128:(u + 1) * 128],
                                               rows[t % 2][:, f0 + u, :], identity[:, :])
                last.then_inc(turned_ready, 1)

            def products(t, half):
                if half == 0:
                    pe.wait_ge(turned_placed, NG * (t + 1))
                if t == 0 and half == 0:
                    pe.wait_ge(dense_placed, 1)
                    pe.wait_ge(picked_placed, PICKED)
                if t >= 1:
                    pe.wait_ge(pairs_act, 2 * t + half - 1)
                    pe.wait_ge(pairs_dve, 2 * t + half - 1)
                for i in range(PER_QUAD):
                    for j in range(QUADS):
                        x = vecs[:, t * TILE + half * HALF + PER_QUAD * j + i, :]
                        last = nc.tensor.matmul(gram[half][32 * j:32 * j + VECS, i * VECS:(i + 1) * VECS],
                                                x, x, start=True, stop=True)
                last.then_inc(gram_ready, 1)

            def layer1(b, slices=range(S1)):
                b0, n = BATCHES[b]
                cols = slice(b0, b0 + n)
                if b == 0:
                    pe.wait_ge(dense_in, 16)
                    pe.wait_ge(w1_in, 16)
                    pe.wait_ge(w1_dense_ready, 1)
                for s in slices:
                    if S1 * b + s >= 2:
                        pe.wait_ge(h1_ready, S1 * b + s - 1)
                    o = slice(s * 128, (s + 1) * 128)
                    out = shared[s % 2][:, (s // 2) * n:(s // 2) * n + n]
                    nc.tensor.matmul(out, w1_dense[:, o], dense[:, cols], start=True, stop=False)
                    if s == 0:
                        pe.wait_ge(pairs_act, (b0 + n) // HALF)
                        pe.wait_ge(pairs_dve, (b0 + n) // HALF)
                    for c in range(CHUNKS):
                        last = nc.tensor.matmul(out, w1[:, c, o], pairs[:, c, cols],
                                                start=False, stop=c == CHUNKS - 1)
                    last.then_inc(h1_sum_ready, 1)

            def layer2(b):
                b0, n = BATCHES[b]
                if b == 0:
                    pe.wait_ge(w2_in, 16)
                else:
                    pe.wait_ge(h2_ready, b)
                for o in range(S2):
                    for s in range(S1):
                        if o == 0:
                            pe.wait_ge(h1_ready, S1 * b + s + 1)
                        last = nc.tensor.matmul(h2_sum[:, o * n:(o + 1) * n],
                                                w2[:, s, o * 128:(o + 1) * 128], h1[:, s, b0 % 256:b0 % 256 + n],
                                                start=s == 0, stop=s == S1 - 1)
                last.then_inc(h2_sum_ready, 1)

            def layer3(b):
                b0, n = BATCHES[b]
                if b == 0:
                    pe.wait_ge(small_in, 48)
                else:
                    pe.wait_ge(y_ready, b)
                pe.wait_ge(h2_ready, b + 1)
                for o in range(S2):
                    last = nc.tensor.matmul(y_sum[0:1, 0:n], w3[:, o:o + 1], h2[:, o, b0 % 256:b0 % 256 + n],
                                            start=o == 0, stop=o == S2 - 1)
                last.then_inc(y_sum_ready, 1)

            pe.wait_ge(blank_zero, 1)
            for _ in range(WARM_UPS):
                nc.tensor.matmul(y_sum[:, :], blank[:, 0:128], blank[:, :], start=True, stop=True)
            for u in range(PICKED):
                pick(u)
                if u == 0:
                    pe.wait_ge(ident_ready, 1)
                for t, g in TURNS_AFTER.get(u, []):
                    turn(t, g)
            products(0, 0)
            turn(1, 3)
            products(0, 1)
            turn(1, 4)
            products(1, 0)
            products(1, 1)
            turn(2, 0)
            turn(2, 1)
            layer1(0, [0, 1])
            turn(2, 2)
            turn(2, 3)
            layer1(0, [2, 3])
            turn(2, 4)
            layer2(0)
            products(2, 0)
            turn(3, 0)
            turn(3, 1)
            products(2, 1)
            turn(3, 2)
            turn(3, 3)
            layer3(0)
            layer1(1, [0, 1])
            turn(3, 4)
            products(3, 0)
            products(3, 1)
            layer1(1, [2, 3])
            layer1(2, [0, 1])
            layer2(1)
            layer1(2, [2, 3])
            layer3(1)
            layer2(2)
            layer3(2)

        def place_pairs(eng, copy, h, js, layer_sem):
            def put(layer, q):
                rows_n, first = LAYERS[q][layer]
                for j in js:
                    src = gram[h % 2][32 * j:32 * j + rows_n, 0:PER_QUAD * VECS]
                    b0 = h * HALF + PER_QUAD * j
                    last = copy(pairs[32 * q:32 * q + rows_n, :, b0:b0 + PER_QUAD],
                                src.rearrange("n (i m) -> n m i", m=VECS)[:, first:first + CHUNKS, :])
                return last
            for q in range(QUADS):
                last = put(0, q)
            last.then_inc(layer_sem, 1)
            eng.wait_ge(layer_sem, 2 * h + 1)
            put(1, 2)
            put(1, 3).then_inc(layer_sem, 1)
            put(1, 0)
            put(1, 1)
            eng.wait_ge(layer_sem, 2 * h + 2)
            put(2, 2)
            return put(2, 3)

        @block.scalar
        def _(act):
            def place_turned(t, g):
                k = t * NG + g
                f0, n = GROUPS[g]
                act.wait_ge(turned_ready, k + 1)
                nc.scalar.copy(vecs[:, t * TILE:(t + 1) * TILE, 1 + f0:1 + f0 + n].rearrange("d b n -> d n b"),
                               turned[k % 2][:, 0:n * 128].rearrange("d (n b) -> d n b", n=n)
                               ).then_inc(turned_placed, 1)

            def find_offset(u):
                act.wait_ge(pick_ids_in[u % 2], 16 * (u // 2 + 1))
                if u >= 2:
                    act.wait_ge(onehot_ready, (PER_PART - 1) * (u - 1))
                nc.scalar.activation(offset[u % 2][:, :], pick_ids[u % 2][:, :], ACT.Identity,
                                     bias=minus_first[:, 0:1]).then_inc(offset_ready, 1)

            def last_chunk(u):
                if u == 0:
                    act.wait_ge(offset_ready, 1)
                else:
                    act.wait_ge(offset_ready, u + 1)
                    act.wait_ge(piece_used, 2 * u)
                    act.wait_ge(last_onehot_ready, u)
                nc.scalar.activation(distance[:, :], offset[u % 2][:, :], ACT.Abs, bias=minus_last[:, 0:1]
                                     ).then_inc(distance_ready, 1)
                act.wait_ge(distance_ready, u + 1)
                nc.scalar.activation(onehot[1][:, PIECE - 1, :], distance[:, :], ACT.Relu, bias=one[:, 0:1], scale=-1.0
                                     ).then_inc(last_onehot_ready, 1)

            def split_table(u):
                act.wait_ge(table_in[u % 2], 16 * (u // 2 + 1))
                if u >= 2:
                    act.wait_ge(piece_used, 2 * (u - 1))
                nc.scalar.copy(table_hi[u % 2][:, :, :], table[u % 2][:, :, :]).then_inc(table_hi_ready, 1)

            def place_picked(u):
                act.wait_ge(piece_used, 2 * (u + 1))
                nc.scalar.copy(vecs[:, :, 1 + GATHERED + u], shared[u % 2][:, :]).then_inc(picked_placed, 1)

            def act_pairs(h):
                act.wait_ge(gram_ready, h + 1)
                place_pairs(act, nc.scalar.copy, h, (0, 2), layer_act).then_inc(pairs_act, 1)

            def relu1(b, slices=range(S1)):
                b0, n = BATCHES[b]
                for s in slices:
                    act.wait_ge(h1_sum_ready, S1 * b + s + 1)
                    nc.scalar.activation(h1[:, s, b0 % 256:b0 % 256 + n], shared[s % 2][:, (s // 2) * n:(s // 2) * n + n],
                                         ACT.Relu, bias=b1[:, s:s + 1]).then_inc(h1_ready, 1)

            load_pick_ids(act, 0)
            act.dma_start(minus_first[:, :], a["minus_first"]).then_inc(first_in, 16)
            act.wait_ge(warm_zero, 3)
            nc.scalar.activation(warm[:, 1:2], warm[:, 0:1], ACT.Relu)
            split_table(0)
            last_chunk(0)
            act.wait_ge(first_in, 16)
            find_offset(1)
            split_table(1)
            act.wait_ge(dense_in, 16)
            nc.scalar.copy(vecs[:, :, 0], dense[:, :]).then_inc(dense_placed, 1)
            find_offset(2)
            for u in range(PICKED):
                if 1 <= u and u + 2 < PICKED:
                    find_offset(u + 2)
                place_picked(u)
                if u + 1 < PICKED:
                    last_chunk(u + 1)
                if u + 2 < PICKED:
                    split_table(u + 2)
                for t, g in TURNS_AFTER.get(u, []):
                    place_turned(t, g)
            act.wait_ge(pairs_zero, 1)
            act_pairs(0)
            place_turned(1, 3)
            place_turned(1, 4)
            act_pairs(1)
            act_pairs(2)
            act_pairs(3)
            place_turned(2, 0)
            place_turned(2, 1)
            act.wait_ge(small_in, 48)
            relu1(0, [0, 1])
            place_turned(2, 2)
            place_turned(2, 3)
            relu1(0, [2, 3])
            place_turned(2, 4)
            act_pairs(4)
            place_turned(3, 0)
            place_turned(3, 1)
            act_pairs(5)
            place_turned(3, 2)
            place_turned(3, 3)
            relu1(1, [0, 1])
            place_turned(3, 4)
            act_pairs(6)
            act_pairs(7)
            relu1(1, [2, 3])
            relu1(2)

        @block.vector
        def _(dve):
            def relu2(b):
                b0, n = BATCHES[b]
                dve.wait_ge(h2_sum_ready, b + 1)
                for o in range(S2):
                    last = nc.vector.tensor_scalar(h2[:, o, b0 % 256:b0 % 256 + n], h2_sum[:, o * n:(o + 1) * n],
                                                   b2[:, o:o + 1], 0.0, ALU.add, ALU.max)
                last.then_inc(h2_ready, 1)

            def place_y(b):
                b0, n = BATCHES[b]
                dve.wait_ge(y_sum_ready, b + 1)
                nc.vector.tensor_copy(y[:, b0:b0 + n], y_sum[0:1, 0:n]).then_inc(y_ready, 1)

            def dve_pairs(h):
                dve.wait_ge(gram_ready, h + 1)
                place_pairs(dve, nc.vector.tensor_copy, h, (1, 3), layer_dve).then_inc(pairs_dve, 1)

            def compare(u, half):
                if u >= 1:
                    dve.wait_ge(piece_used, 2 * (u - 1) + half + 1)
                for k in range(PIECE - half):
                    nc.vector.tensor_scalar(onehot[half][:, k, :], offset[u % 2][:, :], float(half * PIECE + k),
                                            None, ALU.is_equal).then_inc(onehot_ready, 1)

            nc.vector.memset(blank[:, :], 0.0).then_inc(blank_zero, 1)
            nc.vector.memset(warm[:, :], 0.0).then_inc(warm_zero, 1)
            nc.vector.memset(one[:, :], 1.0).then_inc(warm_zero, 1)
            nc.vector.memset(minus_last[:, :], 1.0 - PER_PART).then_inc(warm_zero, 1)
            dve.wait_ge(pick_ids_in[0], 16)
            dve.wait_ge(first_in, 16)
            nc.vector.tensor_scalar(offset[0][:, :], pick_ids[0][:, :], minus_first[:, 0:1], None,
                                    ALU.add).then_inc(offset_ready, 1)
            for u in range(PICKED):
                dve.wait_ge(offset_ready, u + 1)
                compare(u, 0)
                dve.wait_ge(table_hi_ready, u + 1)
                if u >= 2:
                    dve.wait_ge(piece_used, 2 * (u - 1))
                nc.vector.tensor_tensor(table_lo[u % 2][:, :, :], table[u % 2][:, :, :],
                                        table_hi[u % 2][:, :, :].bitcast(fp32), ALU.subtract).then_inc(table_lo_ready, 1)
                compare(u, 1)
                if u == 2:
                    nc.vector.memset(pairs[:, :, :], 0.0).then_inc(pairs_zero, 1)
            dve.wait_ge(w1d_in, 16)
            nc.vector.tensor_tensor(w1_dense[:, :], w1_dense2[:, 0, :], w1_dense2[:, 1, :],
                                    ALU.add).then_inc(w1_dense_ready, 1)
            dve.wait_ge(pairs_zero, 1)
            for h in range(4):
                dve_pairs(h)
            dve.wait_ge(small_in, 48)
            relu2(0)
            dve_pairs(4)
            dve_pairs(5)
            place_y(0)
            dve_pairs(6)
            dve_pairs(7)
            relu2(1)
            place_y(1)
            relu2(2)
            place_y(2)


def kernel(**inputs):
    import numpy as _np
    import concourse.bacc as _bacc
    from concourse import mybir as _mybir
    from concourse.bass_utils import run_bass_kernel_spmd as _run

    x = {k: _np.asarray(v) for k, v in inputs.items()}
    W1 = x["W_top1"]
    row_of = {}
    for n in range(VECS):
        for m in range(n + 1, VECS):
            row_of[n, m] = DIM + len(row_of)
    n_pairs = len(row_of)
    w1_pairs = _np.zeros((128, CHUNKS, HID1), W1.dtype)
    for q in range(QUADS):
        for c in range(CHUNKS):
            for n in range(VECS):
                m = [first for rows_n, first in LAYERS[q] if n < rows_n][-1] + c
                k = row_of.pop((min(n, m), max(n, m)), None)
                if k is not None:
                    w1_pairs[32 * q + n, c] = W1[k]
    assert not row_of
    ids = x["ids"]
    arrays = {
        "ids": ids[:, :GATHERED].reshape(TILES, 128, GATHERED).transpose(1, 0, 2),
        "pick_ids": ids[:, GATHERED:].T,
        "minus_first": -PER_PART * _np.arange(PICK_PARTS, dtype=_np.float32)[:, None],
        "dense_t": x["r_dense_proj"].T,
        "w1_dense": _np.stack([W1[:DIM], W1[DIM + n_pairs:]], axis=1),
        "w1_pairs": w1_pairs,
        "w2": x["W_top2"].reshape(S1, 128, HID2).transpose(1, 0, 2),
        "w3": x["W_top3"].reshape(S2, 128).T,
        "b1": x["b_top1"].reshape(S1, 128).T,
        "b2": x["b_top2"].reshape(S2, 128).T,
    }
    for f in range(TABLES):
        arrays[f"tbl_{f}"] = x[f"tbl_{f}"]
    nc = _bacc.Bacc("TRN2", target_bir_lowering=False, num_devices=1)
    arrays = {k: _np.ascontiguousarray(v) for k, v in arrays.items()}
    aps = {k: nc.dram_tensor(f"in_{k}", v.shape, _mybir.dt.from_np(v.dtype), kind="ExternalInput").ap()
           for k, v in arrays.items()}
    y_out = nc.dram_tensor("out_y", (BATCH, 1), _mybir.dt.float32, kind="ExternalOutput").ap()
    build_dlrm(nc, aps, y_out.rearrange("b o -> o b"))
    r = _run(nc, [{f"in_{k}": v for k, v in arrays.items()}], core_ids=[0])
    return r.results[0]["out_y"]
```

```python
import concourse.bass as bass
from concourse import mybir
from contextlib import ExitStack

BATCH = 512
DIM = 128
TABLES = 26
VECS = TABLES + 1
TILE = 128
TILES = BATCH // TILE
HALF = TILE // 2
Y_TILES = [(0, 2), (2, 3), (3, 4)]
HID1 = 512
HID2 = 256
S1 = HID1 // 128
S2 = HID2 // 128
QUADS = 4
PER_QUAD = HALF // QUADS
CHUNKS = 4
LAYERS = [[(27, 23), (10, 7)],
          [(27, 0), (14, 11)],
          [(27, 4), (19, 15), (4, 0)],
          [(27, 8), (22, 19), (7, 3)]]
PICK_TABLES = [7, 18, 19, 20, 21, 22, 23, 24, 25]
GATHER_TABLES = [f for f in range(TABLES) if f not in PICK_TABLES]
PICKED = len(PICK_TABLES)
GATHERED = len(GATHER_TABLES)
PICK_ROWS = 1000
PER_PART = 8
PICK_PARTS = PICK_ROWS // PER_PART
PIECE = PER_PART // 2
GROUPS = [(f, min(4, GATHERED - f)) for f in range(0, GATHERED, 4)]
NG = len(GROUPS)
WARM_UPS = 12
TURNS_AFTER = {1: [(0, 0)], 2: [(0, 1)], 3: [(0, 2)], 4: [(0, 3), (0, 4)], 5: [(1, 0)], 6: [(1, 1)], 8: [(1, 2)]}


def build_dlrm(nc, a, y_out):
    fp32 = mybir.dt.float32
    fp32r = mybir.dt.float32r
    fp16 = mybir.dt.float16
    bf16 = mybir.dt.bfloat16
    i32 = mybir.dt.int32
    ALU = mybir.AluOpType
    ACT = mybir.ActivationFunctionType

    ctx = ExitStack()
    with ctx:
        def sb(name, shape, dt=fp32):
            return ctx.enter_context(nc.sbuf_tensor(name, shape, dt))

        def bank(name):
            return ctx.enter_context(nc.psum_tensor(name, [128, 512], fp32))

        def sem(name):
            return ctx.enter_context(nc.semaphore(name))

        ids = sb("ids", [128, TILES, GATHERED], i32)
        rows = [sb(f"rows{i}", [128, GATHERED, DIM]) for i in range(2)]
        vecs = sb("vecs", [128, BATCH, VECS])
        dense = sb("dense", [128, BATCH])
        pairs = sb("pairs", [128, CHUNKS, BATCH])
        w1 = sb("w1", [128, CHUNKS, HID1])
        w1_dense = sb("w1_dense", [128, HID1])
        w1_dense_both = sb("w1_dense_both", [128, 2, HID1])
        w2 = sb("w2", [128, S1, HID2])
        w3 = sb("w3", [128, S2])
        b1 = sb("b1", [128, S1])
        b2 = sb("b2", [128, S2])
        identity = sb("identity", [128, 128])
        h1 = [sb(f"h1_{i}", [128, S1, TILE]) for i in range(2)]
        h2 = sb("h2", [128, S2, BATCH])
        y = sb("y", [1, BATCH])
        minus_first = sb("minus_first", [PICK_PARTS, 1])
        pick_ids = [sb(f"pick_ids{i}", [PICK_PARTS, BATCH], i32) for i in range(2)]
        offset = [sb(f"offset{i}", [PICK_PARTS, BATCH], fp16) for i in range(2)]
        table = [sb(f"table{i}", [PICK_PARTS, PER_PART, DIM]) for i in range(2)]
        table_hi = [sb(f"table_hi{i}", [PICK_PARTS, PER_PART, DIM], fp32r) for i in range(2)]
        table_lo = [sb(f"table_lo{i}", [PICK_PARTS, PER_PART, DIM], fp32r) for i in range(2)]
        distance = sb("distance", [PICK_PARTS, BATCH], fp16)
        act_probe = sb("act_probe", [1, 2])
        blank = sb("blank", [128, 512], bf16)
        one = sb("one", [PICK_PARTS, 1])
        minus_last = sb("minus_last", [PICK_PARTS, 1])
        onehot = [sb(f"onehot{i}", [PICK_PARTS, PIECE, BATCH], fp32r) for i in range(2)]

        turned = [bank(f"turned{i}") for i in range(2)]
        gram = [bank(f"gram{i}") for i in range(2)]
        shared = [bank(f"shared{i}") for i in range(2)]
        h2_sum = [bank(f"h2_sum{i}") for i in range(S2)]
        y_sum = turned[0][0:1, :]

        ids_in = sem("ids_in")
        minus_first_in = sem("minus_first_in")
        dense_in = sem("dense_in")
        w1_in = sem("w1_in")
        w1_dense_in = sem("w1_dense_in")
        w2_in = sem("w2_in")
        small_in = sem("small_in")
        pick_ids_in = [sem(f"pick_ids_in{i}") for i in range(2)]
        table_in = [sem(f"table_in{i}") for i in range(2)]
        rows_in = [[sem(f"rows_in{i}_{g}") for g in range(NG)] for i in range(2)]
        identity_zero = sem("identity_zero")
        identity_ready = sem("identity_ready")
        pairs_zero = sem("pairs_zero")
        w1_dense_ready = sem("w1_dense_ready")
        dense_placed = sem("dense_placed")
        table_hi_ready = sem("table_hi_ready")
        table_lo_ready = sem("table_lo_ready")
        offset_ready = sem("offset_ready")
        onehot_ready = sem("onehot_ready")
        distance_ready = sem("distance_ready")
        last_onehot_ready = sem("last_onehot_ready")
        act_constants_ready = sem("act_constants_ready")
        blank_zero = sem("blank_zero")
        onehot_used = sem("onehot_used")
        picked_placed = sem("picked_placed")
        turned_ready = sem("turned_ready")
        turned_placed = sem("turned_placed")
        gram_ready = sem("gram_ready")
        layer_act = sem("layer_act")
        layer_dve = sem("layer_dve")
        pairs_act = sem("pairs_act")
        pairs_dve = sem("pairs_dve")
        h1_sum_ready = sem("h1_sum_ready")
        h1_ready = sem("h1_ready")
        h2_sum_ready = sem("h2_sum_ready")
        h2_ready = sem("h2_ready")
        y_sum_ready = sem("y_sum_ready")
        y_ready = sem("y_ready")
        y_stored = sem("y_stored")

        block = ctx.enter_context(nc.Block())

        def load_pick_ids(eng, u):
            if u >= 2:
                eng.wait_ge(offset_ready, u - 1)
            eng.dma_start(pick_ids[u % 2][:, :], a["pick_ids"][u:u + 1, :].to_broadcast([PICK_PARTS, BATCH])
                          ).then_inc(pick_ids_in[u % 2], 16)

        def load_table(eng, u):
            if u >= 2:
                eng.wait_ge(table_hi_ready, u - 1)
                eng.wait_ge(table_lo_ready, u - 1)
            eng.dma_start(table[u % 2][:, :, :],
                          a[f"tbl_{PICK_TABLES[u]}"].rearrange("(p r) d -> p r d", r=PER_PART)
                          ).then_inc(table_in[u % 2], 16)

        @block.sync
        def _(sp):
            sp.dma_start(ids[:, :, :], a["ids"]).then_inc(ids_in, 16)
            load_table(sp, 0)
            load_pick_ids(sp, 1)
            load_table(sp, 1)
            sp.dma_start(dense[:, :], a["dense_t"]).then_inc(dense_in, 16)
            for u in range(2, PICKED):
                load_pick_ids(sp, u)
                load_table(sp, u)
            sp.dma_start(w1_dense_both[:, :, :], a["w1_dense"]).then_inc(w1_dense_in, 16)
            sp.dma_start(w1[:, :, :], a["w1_pairs"]).then_inc(w1_in, 16)
            sp.dma_start(b1[:, :], a["b1"]).then_inc(small_in, 16)
            sp.dma_start(b2[:, :], a["b2"]).then_inc(small_in, 16)
            sp.dma_start(w3[:, :], a["w3"]).then_inc(small_in, 16)
            sp.dma_start(w2[:, :, :], a["w2"]).then_inc(w2_in, 16)
            sp.wait_ge(y_ready, len(Y_TILES))
            sp.dma_start(y_out, y[:, :]).then_inc(y_stored, 16)
            sp.wait_ge(y_stored, 16)

        @block.gpsimd
        def _(pool):
            nc.gpsimd.memset(identity[:, :], 0.0).then_inc(identity_zero, 1)
            pool.wait_ge(identity_zero, 1)
            nc.gpsimd.affine_select(out=identity[:, :], in_=identity[:, :], compare_op=ALU.not_equal,
                                    fill=1.0, base=0, pattern=[[-1, 128]],
                                    channel_multiplier=1).then_inc(identity_ready, 1)
            pool.wait_ge(ids_in, 16)
            for t in range(TILES):
                for g, (f0, n) in enumerate(GROUPS):
                    if t >= 2:
                        pool.wait_ge(turned_ready, NG * (t - 2) + g + 1)
                    for f in range(f0, f0 + n):
                        pool.indirect_dma_start(
                            rows[t % 2][:, f, :], None, a[f"tbl_{GATHER_TABLES[f]}"],
                            bass.IndirectOffsetOnAxis(ids[:, t, f:f + 1], 0)).then_inc(rows_in[t % 2][g], 16)

        @block.tensor
        def _(pe):
            def keep_warm(count, free_bank):
                for _ in range(count):
                    nc.tensor.matmul(free_bank[:, :], blank[:, 0:128], blank[:, :], start=True, stop=True)

            def pick(u):
                if u >= 2:
                    pe.wait_ge(picked_placed, u - 1)
                for c0, part in [(0, 0), (0, 1), (PIECE, 0), (PIECE, 1)]:
                    if c0 == 0:
                        pe.wait_ge((table_hi_ready, table_lo_ready)[part], u + 1)
                    for c in range(c0, c0 + PIECE):
                        if part == 0 and c < PER_PART - 1:
                            pe.wait_ge(onehot_ready, (PER_PART - 1) * u + c + 1)
                        elif part == 0:
                            pe.wait_ge(last_onehot_ready, u + 1)
                        last = nc.tensor.matmul(shared[u % 2][:, :], (table_hi, table_lo)[part][u % 2][:, c, :],
                                                onehot[c0 // PIECE][:, c - c0, :],
                                                start=c == 0 and part == 0, stop=c == PER_PART - 1 and part == 1)
                    if part == 1:
                        last.then_inc(onehot_used, 1)

            def turn(t, g):
                k = t * NG + g
                f0, n = GROUPS[g]
                pe.wait_ge(rows_in[t % 2][g], 16 * n * (t // 2 + 1))
                if k >= 2:
                    pe.wait_ge(turned_placed, k - 1)
                for u in range(n):
                    last = nc.tensor.transpose(turned[k % 2][:, u * 128:(u + 1) * 128],
                                               rows[t % 2][:, f0 + u, :], identity[:, :])
                last.then_inc(turned_ready, 1)

            def products(t, half):
                if half == 0:
                    pe.wait_ge(turned_placed, NG * (t + 1))
                if t == 0 and half == 0:
                    pe.wait_ge(dense_placed, 1)
                    pe.wait_ge(picked_placed, PICKED)
                if t >= 1:
                    pe.wait_ge(pairs_act, 2 * t + half - 1)
                    pe.wait_ge(pairs_dve, 2 * t + half - 1)
                for i in range(PER_QUAD):
                    for j in range(QUADS):
                        x = vecs[:, t * TILE + half * HALF + PER_QUAD * j + i, :]
                        last = nc.tensor.matmul(gram[half][32 * j:32 * j + VECS, i * VECS:(i + 1) * VECS],
                                                x, x, start=True, stop=True)
                last.then_inc(gram_ready, 1)

            def layer1(t, slices=range(S1)):
                cols = slice(t * TILE, (t + 1) * TILE)
                if t == 0:
                    pe.wait_ge(dense_in, 16)
                    pe.wait_ge(w1_in, 16)
                    pe.wait_ge(w1_dense_ready, 1)
                for s in slices:
                    if S1 * t + s >= 2:
                        pe.wait_ge(h1_ready, S1 * t + s - 1)
                    o = slice(s * 128, (s + 1) * 128)
                    out = shared[s % 2][:, 0:TILE]
                    nc.tensor.matmul(out, w1_dense[:, o], dense[:, cols], start=True, stop=False)
                    if s == 0:
                        pe.wait_ge(pairs_act, 2 * (t + 1))
                        pe.wait_ge(pairs_dve, 2 * (t + 1))
                    for c in range(CHUNKS):
                        last = nc.tensor.matmul(out, w1[:, c, o], pairs[:, c, cols],
                                                start=False, stop=c == CHUNKS - 1)
                    last.then_inc(h1_sum_ready, 1)

            def layer2(t):
                if t == 0:
                    pe.wait_ge(w2_in, 16)
                else:
                    pe.wait_ge(h2_ready, S2 * t)
                for o in range(S2):
                    for s in range(S1):
                        if o == 0:
                            pe.wait_ge(h1_ready, S1 * t + s + 1)
                        last = nc.tensor.matmul(h2_sum[o][:, 0:TILE], w2[:, s, o * 128:(o + 1) * 128],
                                                h1[t % 2][:, s, :], start=s == 0, stop=s == S1 - 1)
                    last.then_inc(h2_sum_ready, 1)

            def layer3(k):
                t0, t1 = Y_TILES[k]
                if k == 0:
                    pe.wait_ge(small_in, 48)
                else:
                    pe.wait_ge(y_ready, k)
                cols = slice(t0 * TILE, t1 * TILE)
                for o in range(S2):
                    pe.wait_ge(h2_ready, S2 * (t1 - 1) + o + 1)
                    last = nc.tensor.matmul(y_sum[:, cols], w3[:, o:o + 1], h2[:, o, cols],
                                            start=o == 0, stop=o == S2 - 1)
                last.then_inc(y_sum_ready, 1)

            pe.wait_ge(blank_zero, 1)
            keep_warm(WARM_UPS, h2_sum[1])

            for u in range(PICKED):
                pick(u)
                if u == 0:
                    pe.wait_ge(identity_ready, 1)
                for t, g in TURNS_AFTER.get(u, []):
                    turn(t, g)
            products(0, 0)
            turn(1, 3)
            products(0, 1)
            turn(1, 4)
            keep_warm(2, h2_sum[1])
            products(1, 0)
            turn(2, 0)
            keep_warm(2, h2_sum[1])
            layer1(0, [0])
            products(1, 1)
            layer1(0, [1])
            turn(2, 1)
            layer1(0, [2])
            turn(2, 2)
            layer1(0, [3])
            turn(2, 3)
            layer1(1, [0])
            turn(2, 4)
            layer1(1, [1])
            products(2, 0)
            layer2(0)
            products(2, 1)
            layer1(1, [2, 3])
            turn(3, 0)
            turn(3, 1)
            layer1(2, [0, 1])
            turn(3, 2)
            layer2(1)
            turn(3, 3)
            turn(3, 4)
            layer1(2, [2])
            pe.wait_ge(h2_ready, 2 * S2)
            keep_warm(1, h2_sum[1])
            products(3, 0)
            layer1(2, [3])
            products(3, 1)
            layer2(2)
            pe.wait_ge(turned_placed, NG * TILES)
            layer3(0)
            keep_warm(1, turned[1])
            layer1(3)
            layer3(1)
            layer2(3)
            layer3(2)

        def place_pairs(eng, copy, h, js, layer_sem):
            def put(layer, q):
                rows_n, first = LAYERS[q][layer]
                for j in js:
                    src = gram[h % 2][32 * j:32 * j + rows_n, 0:PER_QUAD * VECS]
                    b0 = h * HALF + PER_QUAD * j
                    last = copy(pairs[32 * q:32 * q + rows_n, :, b0:b0 + PER_QUAD],
                                src.rearrange("n (i m) -> n m i", m=VECS)[:, first:first + CHUNKS, :])
                return last
            for q in range(QUADS):
                last = put(0, q)
            last.then_inc(layer_sem, 1)
            eng.wait_ge(layer_sem, 2 * h + 1)
            put(1, 2)
            put(1, 3).then_inc(layer_sem, 1)
            put(1, 0)
            put(1, 1)
            eng.wait_ge(layer_sem, 2 * h + 2)
            put(2, 2)
            return put(2, 3)

        @block.scalar
        def _(act):
            def place_turned(t, g):
                k = t * NG + g
                f0, n = GROUPS[g]
                act.wait_ge(turned_ready, k + 1)
                nc.scalar.copy(vecs[:, t * TILE:(t + 1) * TILE, 1 + f0:1 + f0 + n].rearrange("d b n -> d n b"),
                               turned[k % 2][:, 0:n * 128].rearrange("d (n b) -> d n b", n=n)
                               ).then_inc(turned_placed, 1)

            def find_offset(u):
                act.wait_ge(pick_ids_in[u % 2], 16 * (u // 2 + 1))
                if u >= 2:
                    act.wait_ge(onehot_ready, (PER_PART - 1) * (u - 1))
                    act.wait_ge(distance_ready, u - 1)
                nc.scalar.activation(offset[u % 2][:, :], pick_ids[u % 2][:, :], ACT.Identity,
                                     bias=minus_first[:, 0:1]).then_inc(offset_ready, 1)

            def find_distance(u):
                act.wait_ge(offset_ready, u + 1)
                if u >= 1:
                    act.wait_ge(last_onehot_ready, u)
                nc.scalar.activation(distance[:, :], offset[u % 2][:, :], ACT.Abs, bias=minus_last[:, 0:1]
                                     ).then_inc(distance_ready, 1)

            def last_chunk(u):
                if u >= 1:
                    act.wait_ge(onehot_used, 2 * u)
                act.wait_ge(distance_ready, u + 1)
                nc.scalar.activation(onehot[1][:, PIECE - 1, :], distance[:, :], ACT.Relu, bias=one[:, 0:1], scale=-1.0
                                     ).then_inc(last_onehot_ready, 1)

            def split_table(u):
                act.wait_ge(table_in[u % 2], 16 * (u // 2 + 1))
                if u >= 2:
                    act.wait_ge(onehot_used, 2 * (u - 1))
                nc.scalar.copy(table_hi[u % 2][:, :, :], table[u % 2][:, :, :]).then_inc(table_hi_ready, 1)

            def place_picked(u):
                act.wait_ge(onehot_used, 2 * (u + 1))
                nc.scalar.copy(vecs[:, :, 1 + GATHERED + u], shared[u % 2][:, :]).then_inc(picked_placed, 1)

            def act_pairs(h):
                act.wait_ge(gram_ready, h + 1)
                place_pairs(act, nc.scalar.copy, h, (0, 2), layer_act).then_inc(pairs_act, 1)

            def relu1(t, slices=range(S1)):
                if t >= 2:
                    act.wait_ge(h2_sum_ready, S2 * (t - 1))
                for s in slices:
                    act.wait_ge(h1_sum_ready, S1 * t + s + 1)
                    nc.scalar.activation(h1[t % 2][:, s, :], shared[s % 2][:, 0:TILE],
                                         ACT.Relu, bias=b1[:, s:s + 1]).then_inc(h1_ready, 1)

            load_pick_ids(act, 0)
            act.dma_start(minus_first[:, :], a["minus_first"]).then_inc(minus_first_in, 16)
            act.wait_ge(act_constants_ready, 3)
            nc.scalar.activation(act_probe[:, 1:2], act_probe[:, 0:1], ACT.Relu)
            split_table(0)
            find_distance(0)
            last_chunk(0)
            act.wait_ge(minus_first_in, 16)
            find_offset(1)
            split_table(1)
            find_distance(1)
            find_offset(2)
            act.wait_ge(dense_in, 16)
            nc.scalar.copy(vecs[:, :, 0], dense[:, :]).then_inc(dense_placed, 1)
            for u in range(PICKED):
                if u + 1 < PICKED:
                    last_chunk(u + 1)
                if u + 2 < PICKED:
                    split_table(u + 2)
                place_picked(u)
                if u + 3 < PICKED:
                    find_offset(u + 3)
                if u + 2 < PICKED:
                    find_distance(u + 2)
                for t, g in TURNS_AFTER.get(u, []):
                    place_turned(t, g)
            act.wait_ge(pairs_zero, 1)
            act_pairs(0)
            place_turned(1, 3)
            place_turned(1, 4)
            act_pairs(1)
            place_turned(2, 0)
            act.wait_ge(small_in, 48)
            act_pairs(2)
            relu1(0, [0])
            act_pairs(3)
            relu1(0, [1])
            place_turned(2, 1)
            relu1(0, [2])
            place_turned(2, 2)
            relu1(0, [3])
            place_turned(2, 3)
            relu1(1, [0])
            place_turned(2, 4)
            relu1(1, [1])
            act_pairs(4)
            act_pairs(5)
            relu1(1, [2, 3])
            place_turned(3, 0)
            place_turned(3, 1)
            relu1(2, [0, 1])
            place_turned(3, 2)
            place_turned(3, 3)
            place_turned(3, 4)
            relu1(2, [2])
            act_pairs(6)
            relu1(2, [3])
            act_pairs(7)
            relu1(3)

        @block.vector
        def _(dve):
            def relu2(t):
                for o in range(S2):
                    dve.wait_ge(h2_sum_ready, S2 * t + o + 1)
                    nc.vector.tensor_scalar(h2[:, o, t * TILE:(t + 1) * TILE], h2_sum[o][:, 0:TILE],
                                            b2[:, o:o + 1], 0.0, ALU.add, ALU.max).then_inc(h2_ready, 1)

            def place_y(k):
                dve.wait_ge(y_sum_ready, k + 1)
                cols = slice(Y_TILES[k][0] * TILE, Y_TILES[k][1] * TILE)
                nc.vector.tensor_copy(y[:, cols], y_sum[:, cols]).then_inc(y_ready, 1)

            def dve_pairs(h):
                dve.wait_ge(gram_ready, h + 1)
                place_pairs(dve, nc.vector.tensor_copy, h, (1, 3), layer_dve).then_inc(pairs_dve, 1)

            def make_low(u):
                dve.wait_ge(table_hi_ready, u + 1)
                if u >= 2:
                    dve.wait_ge(onehot_used, 2 * (u - 1))
                nc.vector.tensor_tensor(table_lo[u % 2][:, :, :], table[u % 2][:, :, :],
                                        table_hi[u % 2][:, :, :].bitcast(fp32), ALU.subtract
                                        ).then_inc(table_lo_ready, 1)

            def compare(u, half):
                if u >= 1:
                    dve.wait_ge(onehot_used, 2 * (u - 1) + half + 1)
                for k in range(PIECE - half):
                    nc.vector.tensor_scalar(onehot[half][:, k, :], offset[u % 2][:, :], float(half * PIECE + k),
                                            None, ALU.is_equal).then_inc(onehot_ready, 1)

            nc.vector.memset(blank[:, :], 0.0).then_inc(blank_zero, 1)
            nc.vector.memset(act_probe[:, :], 0.0).then_inc(act_constants_ready, 1)
            nc.vector.memset(one[:, :], 1.0).then_inc(act_constants_ready, 1)
            nc.vector.memset(minus_last[:, :], 1.0 - PER_PART).then_inc(act_constants_ready, 1)
            nc.vector.memset(pairs[:, :, :], 0.0).then_inc(pairs_zero, 1)
            dve.wait_ge(pick_ids_in[0], 16)
            dve.wait_ge(minus_first_in, 16)
            nc.vector.tensor_scalar(offset[0][:, :], pick_ids[0][:, :], minus_first[:, 0:1], None,
                                    ALU.add).then_inc(offset_ready, 1)
            dve.wait_ge(offset_ready, 1)
            compare(0, 0)
            make_low(0)
            compare(0, 1)
            for u in range(1, PICKED):
                make_low(u)
                dve.wait_ge(offset_ready, u + 1)
                compare(u, 0)
                compare(u, 1)
            dve.wait_ge(w1_dense_in, 16)
            nc.vector.tensor_tensor(w1_dense[:, :], w1_dense_both[:, 0, :], w1_dense_both[:, 1, :],
                                    ALU.add).then_inc(w1_dense_ready, 1)
            dve.wait_ge(pairs_zero, 1)
            for h in range(5):
                dve_pairs(h)
            dve.wait_ge(small_in, 48)
            relu2(0)
            dve_pairs(5)
            relu2(1)
            dve_pairs(6)
            dve_pairs(7)
            relu2(2)
            place_y(0)
            place_y(1)
            relu2(3)
            place_y(2)


def kernel(**inputs):
    import numpy as _np
    import concourse.bacc as _bacc
    from concourse import mybir as _mybir
    from concourse.bass_utils import run_bass_kernel_spmd as _run

    x = {k: _np.asarray(v) for k, v in inputs.items()}
    W1 = x["W_top1"]
    number = [0] + [1 + f for f in GATHER_TABLES + PICK_TABLES]
    row_of = {}
    for n in range(VECS):
        for m in range(n + 1, VECS):
            row_of[n, m] = DIM + len(row_of)
    n_pairs = len(row_of)
    w1_pairs = _np.zeros((128, CHUNKS, HID1), W1.dtype)
    for q in range(QUADS):
        for c in range(CHUNKS):
            for n in range(VECS):
                m = [first for rows_n, first in LAYERS[q] if n < rows_n][-1] + c
                k = row_of.pop(tuple(sorted((number[n], number[m]))), None)
                if k is not None:
                    w1_pairs[32 * q + n, c] = W1[k]
    assert not row_of
    ids = x["ids"]
    arrays = {
        "ids": ids[:, GATHER_TABLES].reshape(TILES, 128, GATHERED).transpose(1, 0, 2),
        "pick_ids": ids[:, PICK_TABLES].T,
        "minus_first": -PER_PART * _np.arange(PICK_PARTS, dtype=_np.float32)[:, None],
        "dense_t": x["r_dense_proj"].T,
        "w1_dense": _np.stack([W1[:DIM], W1[DIM + n_pairs:]], axis=1),
        "w1_pairs": w1_pairs,
        "w2": x["W_top2"].reshape(S1, 128, HID2).transpose(1, 0, 2),
        "w3": x["W_top3"].reshape(S2, 128).T,
        "b1": x["b_top1"].reshape(S1, 128).T,
        "b2": x["b_top2"].reshape(S2, 128).T,
    }
    for f in range(TABLES):
        arrays[f"tbl_{f}"] = x[f"tbl_{f}"]
    nc = _bacc.Bacc("TRN2", target_bir_lowering=False, num_devices=1)
    arrays = {k: _np.ascontiguousarray(v) for k, v in arrays.items()}
    aps = {k: nc.dram_tensor(f"in_{k}", v.shape, _mybir.dt.from_np(v.dtype), kind="ExternalInput").ap()
           for k, v in arrays.items()}
    y_out = nc.dram_tensor("out_y", (BATCH, 1), _mybir.dt.float32, kind="ExternalOutput").ap()
    build_dlrm(nc, aps, y_out.rearrange("b o -> o b"))
    r = _run(nc, [{f"in_{k}": v for k, v in arrays.items()}], core_ids=[0])
    return r.results[0]["out_y"]
```
